# Optimizing a Trainium2 kernel written in Bass

```python
import numpy as np
import jax
import jax.numpy as jnp

def _softmax(x, axis=-1):
    return jax.nn.softmax(x, axis=axis)

def _gelu(x):
    return jax.nn.gelu(x, approximate=True)

def _silu(x):
    return jax.nn.silu(x)

def _sigmoid(x):
    return jax.nn.sigmoid(x)

def _layernorm(x, axis=-1, eps=1e-05):
    m = jnp.mean(x, axis=axis, keepdims=True)
    v = jnp.var(x, axis=axis, keepdims=True)
    return (x - m) / jnp.sqrt(v + eps)

def _scatter_add(tgt, idx, src, axis=0):
    return tgt.at[idx].add(src)

def _segment_sum(src, seg, n):
    return jax.ops.segment_sum(src, seg, n)
kernel_name = 'mk_conv_preact_d4_conv_nchw64_r2_9d4c15'

def setup_inputs(seed: int=0):
    np.random.seed(seed)
    _w = jnp.asarray

    def _rec_inputs():
        import jax
        import jax.numpy as jnp
        _gk = jax.random.key(seed)
        x = -0.0005207 + 1.001 * jax.random.normal(jax.random.fold_in(_gk, 1), (2, 32, 64, 64), jnp.float32)
        return x
    x = _rec_inputs()

    def _L0_conv_setup():
        import jax, jax.numpy as jnp
        import numpy as np
        BN_EPS = 1e-05

        def conv3x3(x, w, b):
            y = jax.lax.conv_general_dilated(x, w, (1, 1), ((1, 1), (1, 1)), dimension_numbers=('NCHW', 'OIHW', 'NCHW'))
            return y + b[None, :, None, None]

        def bilinear_sample(x, py, px):
            B, C, H, W = x.shape
            y0 = jnp.floor(py)
            x0 = jnp.floor(px)
            wy1 = py - y0
            wx1 = px - x0

            def corner(yc, xc, wgt):
                valid = (yc >= 0) & (yc <= H - 1) & (xc >= 0) & (xc <= W - 1)
                yi = jnp.clip(yc, 0, H - 1).astype(jnp.int32)
                xi = jnp.clip(xc, 0, W - 1).astype(jnp.int32)
                g = jax.vmap(lambda img, yy, xx: img[:, yy, xx])(x, yi, xi)
                return g * jnp.where(valid, wgt, 0.0)[:, None]
            return corner(y0, x0, (1 - wy1) * (1 - wx1)) + corner(y0, x0 + 1, (1 - wy1) * wx1) + corner(y0 + 1, x0, wy1 * (1 - wx1)) + corner(y0 + 1, x0 + 1, wy1 * wx1)

        def deform_conv(x, conv_w, off_w, off_b, mask_w, mask_b, gamma, beta):
            B, C, H, W = x.shape
            O = conv_w.shape[0]
            offset = conv3x3(x, off_w, off_b)
            mask = jax.nn.sigmoid(conv3x3(x, mask_w, mask_b))
            off = offset.reshape(B, 9, 2, H, W)
            ky = jnp.repeat(jnp.arange(3), 3).astype(x.dtype)
            kx = jnp.tile(jnp.arange(3), 3).astype(x.dtype)
            gy = jnp.arange(H, dtype=x.dtype)
            gx = jnp.arange(W, dtype=x.dtype)
            py = off[:, :, 0] + gy[None, None, :, None] + (ky - 1.0)[None, :, None, None]
            px = off[:, :, 1] + gx[None, None, None, :] + (kx - 1.0)[None, :, None, None]
            val = bilinear_sample(x, py, px)
            val = val * mask[:, None]
            out = jnp.einsum('bckhw,ock->bohw', val, conv_w.reshape(O, C, 9))
            mean = out.mean(axis=(0, 2, 3))
            var = out.var(axis=(0, 2, 3))
            out = (out - mean[None, :, None, None]) * jax.lax.rsqrt(var + BN_EPS)[None, :, None, None]
            out = out * gamma[None, :, None, None] + beta[None, :, None, None]
            return jax.nn.relu(out)
        key = jax.random.key(seed)
        ks = jax.random.split(key, 8)
        B, Cin, Cout, H, W = (2, 32, 32, 64, 64)
        x = jax.random.normal(ks[0], (B, Cin, H, W), dtype=jnp.float32)
        fan = Cin * 9
        conv_w = jax.random.normal(ks[1], (Cout, Cin, 3, 3), dtype=jnp.float32) / np.sqrt(fan)
        off_w = jax.random.normal(ks[2], (18, Cin, 3, 3), dtype=jnp.float32) * 0.01
        off_b = jax.random.normal(ks[3], (18,), dtype=jnp.float32) * 0.1
        mask_w = jax.random.normal(ks[4], (9, Cin, 3, 3), dtype=jnp.float32) * 0.01
        mask_b = jnp.zeros((9,), dtype=jnp.float32)
        gamma = jnp.ones((Cout,), dtype=jnp.float32)
        beta = jnp.zeros((Cout,), dtype=jnp.float32)
        return {'x': x, 'conv_w': conv_w, 'off_w': off_w, 'off_b': off_b, 'mask_w': mask_w, 'mask_b': mask_b, 'gamma': gamma, 'beta': beta}
    _L0_conv_all = _L0_conv_setup()
    _L0_conv_in = {k: v for k, v in _L0_conv_all.items() if k in ('conv_w', 'off_w', 'off_b', 'mask_w', 'mask_b', 'gamma', 'beta')}
    del _L0_conv_all

    def _L1_conv_setup():
        import jax, jax.numpy as jnp
        import numpy as np
        B, C_IN, C_OUT, H, W = (32, 32, 32, 56, 56)

        def sign_ste(x, alpha):
            est = jnp.tanh(alpha * x)
            return jax.lax.stop_gradient(jnp.sign(x) - est) + est
        key = jax.random.key(seed)
        kx, kw = jax.random.split(key)
        x = jax.random.normal(kx, (B, C_IN, H, W), dtype=jnp.float32)
        weight = jax.random.normal(kw, (C_OUT, C_IN, 1, 1), dtype=jnp.float32)
        alpha_x = jnp.array(1.0, dtype=jnp.float32)
        alpha_w = jnp.array(1.0, dtype=jnp.float32)
        return {'x': x, 'weight': weight, 'alpha_x': alpha_x, 'alpha_w': alpha_w}
    _L1_conv_all = _L1_conv_setup()
    _L1_conv_in = {k: v for k, v in _L1_conv_all.items() if k in ('weight', 'alpha_x', 'alpha_w')}
    del _L1_conv_all

    def _L2_conv_setup():
        import jax, jax.numpy as jnp
        import numpy as np
        K = 3
        PAD = 1
        STRIDE = 1

        def conv2d(x, w, b):
            y = jax.lax.conv_general_dilated(x, w, window_strides=(STRIDE, STRIDE), padding=((PAD, PAD), (PAD, PAD)), dimension_numbers=('NCHW', 'OIHW', 'NCHW'))
            return y + b[None, :, None, None]

        def deform_conv(x, offset, w, b):
            B, C, H, W = x.shape
            Ho, Wo = (offset.shape[2], offset.shape[3])
            KK = K * K
            oy = offset[:, 0::2]
            ox = offset[:, 1::2]
            ky = jnp.repeat(jnp.arange(K, dtype=x.dtype), K)
            kx = jnp.tile(jnp.arange(K, dtype=x.dtype), K)
            base_y = jnp.arange(Ho, dtype=x.dtype) * STRIDE - PAD
            base_x = jnp.arange(Wo, dtype=x.dtype) * STRIDE - PAD
            ys = base_y[None, None, :, None] + ky[None, :, None, None] + oy
            xs = base_x[None, None, None, :] + kx[None, :, None, None] + ox

            def sample_one(xf, ys_b, xs_b):
                y0 = jnp.floor(ys_b)
                x0 = jnp.floor(xs_b)
                dy = ys_b - y0
                dx = xs_b - x0
                y0i = y0.astype(jnp.int32)
                x0i = x0.astype(jnp.int32)
                acc = jnp.zeros((C, KK, Ho, Wo), dtype=xf.dtype)
                corners = [(y0i, x0i, (1 - dy) * (1 - dx)), (y0i, x0i + 1, (1 - dy) * dx), (y0i + 1, x0i, dy * (1 - dx)), (y0i + 1, x0i + 1, dy * dx)]
                for yi, xi, wgt in corners:
                    valid = ((yi >= 0) & (yi < H) & (xi >= 0) & (xi < W)).astype(xf.dtype)
                    idx = jnp.clip(yi, 0, H - 1) * W + jnp.clip(xi, 0, W - 1)
                    v = jnp.take(xf, idx.reshape(-1), axis=1).reshape(C, KK, Ho, Wo)
                    acc = acc + v * (wgt * valid)[None]
                return acc
            vals = jax.vmap(sample_one)(x.reshape(B, C, H * W), ys, xs)
            out = jnp.einsum('bckhw,ock->bohw', vals, w.reshape(w.shape[0], C, KK))
            return out + b[None, :, None, None]
        key = jax.random.key(seed)
        k1, k2, k3, k4, k5 = jax.random.split(key, 5)
        B, C, H, W = (8, 32, 64, 64)
        Cout = 32
        x = jax.random.normal(k1, (B, C, H, W), dtype=jnp.float32)
        offset_w = jax.random.normal(k2, (2 * K * K, C, K, K), dtype=jnp.float32) * 0.05
        offset_b = jnp.zeros((2 * K * K,), dtype=jnp.float32)
        deform_w = jax.random.normal(k3, (Cout, C, K, K), dtype=jnp.float32) * (1.0 / np.sqrt(C * K * K))
        deform_b = jax.random.normal(k4, (Cout,), dtype=jnp.float32) * 0.01
        return {'x': x, 'offset_w': offset_w, 'offset_b': offset_b, 'deform_w': deform_w, 'deform_b': deform_b}
    _L2_conv_all = _L2_conv_setup()
    _L2_conv_in = {k: v for k, v in _L2_conv_all.items() if k in ('offset_w', 'offset_b', 'deform_w', 'deform_b')}
    del _L2_conv_all

    def _L3_conv_setup():
        import jax, jax.numpy as jnp
        import numpy as np
        B, C, H, W = (4, 32, 32, 32)
        key = jax.random.key(seed)
        k = jax.random.split(key, 7)
        s = 1.0 / np.sqrt(C)
        return {'x': jax.random.normal(k[0], (B, C, H, W), dtype=jnp.float32), 'w1': jax.random.normal(k[1], (C, C), dtype=jnp.float32) * s, 'b1': jax.random.normal(k[2], (C,), dtype=jnp.float32) * 0.01, 'w2': jax.random.normal(k[3], (C, C), dtype=jnp.float32) * s, 'b2': jax.random.normal(k[4], (C,), dtype=jnp.float32) * 0.01, 'w3': jax.random.normal(k[5], (C, C), dtype=jnp.float32) * s, 'b3': jax.random.normal(k[6], (C,), dtype=jnp.float32) * 0.01}
    _L3_conv_all = _L3_conv_setup()
    _L3_conv_in = {k: v for k, v in _L3_conv_all.items() if k in ('w1', 'b1', 'w2', 'b2', 'w3', 'b3')}
    del _L3_conv_all
    return {'x': x, 'L0_conv_conv_w': _L0_conv_in['conv_w'], 'L0_conv_off_w': _L0_conv_in['off_w'], 'L0_conv_off_b': _L0_conv_in['off_b'], 'L0_conv_mask_w': _L0_conv_in['mask_w'], 'L0_conv_mask_b': _L0_conv_in['mask_b'], 'L0_conv_gamma': _L0_conv_in['gamma'], 'L0_conv_beta': _L0_conv_in['beta'], 'L1_conv_weight': _L1_conv_in['weight'], 'L1_conv_alpha_x': _L1_conv_in['alpha_x'], 'L1_conv_alpha_w': _L1_conv_in['alpha_w'], 'L2_conv_offset_w': _L2_conv_in['offset_w'], 'L2_conv_offset_b': _L2_conv_in['offset_b'], 'L2_conv_deform_w': _L2_conv_in['deform_w'], 'L2_conv_deform_b': _L2_conv_in['deform_b'], 'L3_conv_w1': _L3_conv_in['w1'], 'L3_conv_b1': _L3_conv_in['b1'], 'L3_conv_w2': _L3_conv_in['w2'], 'L3_conv_b2': _L3_conv_in['b2'], 'L3_conv_w3': _L3_conv_in['w3'], 'L3_conv_b3': _L3_conv_in['b3']}

def reference(x, L0_conv_conv_w, L0_conv_off_w, L0_conv_off_b, L0_conv_mask_w, L0_conv_mask_b, L0_conv_gamma, L0_conv_beta, L1_conv_weight, L1_conv_alpha_x, L1_conv_alpha_w, L2_conv_offset_w, L2_conv_offset_b, L2_conv_deform_w, L2_conv_deform_b, L3_conv_w1, L3_conv_b1, L3_conv_w2, L3_conv_b2, L3_conv_w3, L3_conv_b3):
    import jax
    import jax.numpy as jnp

    def _L0_conv_ref(x, conv_w, off_w, off_b, mask_w, mask_b, gamma, beta):
        import jax, jax.numpy as jnp
        import numpy as np
        BN_EPS = 1e-05

        def conv3x3(x, w, b):
            y = jax.lax.conv_general_dilated(x, w, (1, 1), ((1, 1), (1, 1)), dimension_numbers=('NCHW', 'OIHW', 'NCHW'))
            return y + b[None, :, None, None]

        def bilinear_sample(x, py, px):
            B, C, H, W = x.shape
            y0 = jnp.floor(py)
            x0 = jnp.floor(px)
            wy1 = py - y0
            wx1 = px - x0

            def corner(yc, xc, wgt):
                valid = (yc >= 0) & (yc <= H - 1) & (xc >= 0) & (xc <= W - 1)
                yi = jnp.clip(yc, 0, H - 1).astype(jnp.int32)
                xi = jnp.clip(xc, 0, W - 1).astype(jnp.int32)
                g = jax.vmap(lambda img, yy, xx: img[:, yy, xx])(x, yi, xi)
                return g * jnp.where(valid, wgt, 0.0)[:, None]
            return corner(y0, x0, (1 - wy1) * (1 - wx1)) + corner(y0, x0 + 1, (1 - wy1) * wx1) + corner(y0 + 1, x0, wy1 * (1 - wx1)) + corner(y0 + 1, x0 + 1, wy1 * wx1)

        def deform_conv(x, conv_w, off_w, off_b, mask_w, mask_b, gamma, beta):
            B, C, H, W = x.shape
            O = conv_w.shape[0]
            offset = conv3x3(x, off_w, off_b)
            mask = jax.nn.sigmoid(conv3x3(x, mask_w, mask_b))
            off = offset.reshape(B, 9, 2, H, W)
            ky = jnp.repeat(jnp.arange(3), 3).astype(x.dtype)
            kx = jnp.tile(jnp.arange(3), 3).astype(x.dtype)
            gy = jnp.arange(H, dtype=x.dtype)
            gx = jnp.arange(W, dtype=x.dtype)
            py = off[:, :, 0] + gy[None, None, :, None] + (ky - 1.0)[None, :, None, None]
            px = off[:, :, 1] + gx[None, None, None, :] + (kx - 1.0)[None, :, None, None]
            val = bilinear_sample(x, py, px)
            val = val * mask[:, None]
            out = jnp.einsum('bckhw,ock->bohw', val, conv_w.reshape(O, C, 9))
            mean = out.mean(axis=(0, 2, 3))
            var = out.var(axis=(0, 2, 3))
            out = (out - mean[None, :, None, None]) * jax.lax.rsqrt(var + BN_EPS)[None, :, None, None]
            out = out * gamma[None, :, None, None] + beta[None, :, None, None]
            return jax.nn.relu(out)
        return deform_conv(x, conv_w, off_w, off_b, mask_w, mask_b, gamma, beta)

    def _L1_conv_ref(x, weight, alpha_x, alpha_w):
        import jax, jax.numpy as jnp
        import numpy as np
        B, C_IN, C_OUT, H, W = (32, 32, 32, 56, 56)

        def sign_ste(x, alpha):
            est = jnp.tanh(alpha * x)
            return jax.lax.stop_gradient(jnp.sign(x) - est) + est
        b, c, h, w = x.shape
        out_ch = weight.shape[0]
        x_unf = x.reshape(b, c, h * w).transpose(0, 2, 1)
        w_unf = weight.reshape(out_ch, c).T
        signxw = jnp.einsum('blc,co->blo', sign_ste(x_unf, alpha_x), w_unf)
        signwx = jnp.einsum('blc,co->blo', x_unf, sign_ste(w_unf, alpha_w))
        out = (signxw + signwx).transpose(0, 2, 1).reshape(b, out_ch, h, w)
        return out

    def _L2_conv_ref(x, offset_w, offset_b, deform_w, deform_b):
        import jax, jax.numpy as jnp
        import numpy as np
        K = 3
        PAD = 1
        STRIDE = 1

        def conv2d(x, w, b):
            y = jax.lax.conv_general_dilated(x, w, window_strides=(STRIDE, STRIDE), padding=((PAD, PAD), (PAD, PAD)), dimension_numbers=('NCHW', 'OIHW', 'NCHW'))
            return y + b[None, :, None, None]

        def deform_conv(x, offset, w, b):
            B, C, H, W = x.shape
            Ho, Wo = (offset.shape[2], offset.shape[3])
            KK = K * K
            oy = offset[:, 0::2]
            ox = offset[:, 1::2]
            ky = jnp.repeat(jnp.arange(K, dtype=x.dtype), K)
            kx = jnp.tile(jnp.arange(K, dtype=x.dtype), K)
            base_y = jnp.arange(Ho, dtype=x.dtype) * STRIDE - PAD
            base_x = jnp.arange(Wo, dtype=x.dtype) * STRIDE - PAD
            ys = base_y[None, None, :, None] + ky[None, :, None, None] + oy
            xs = base_x[None, None, None, :] + kx[None, :, None, None] + ox

            def sample_one(xf, ys_b, xs_b):
                y0 = jnp.floor(ys_b)
                x0 = jnp.floor(xs_b)
                dy = ys_b - y0
                dx = xs_b - x0
                y0i = y0.astype(jnp.int32)
                x0i = x0.astype(jnp.int32)
                acc = jnp.zeros((C, KK, Ho, Wo), dtype=xf.dtype)
                corners = [(y0i, x0i, (1 - dy) * (1 - dx)), (y0i, x0i + 1, (1 - dy) * dx), (y0i + 1, x0i, dy * (1 - dx)), (y0i + 1, x0i + 1, dy * dx)]
                for yi, xi, wgt in corners:
                    valid = ((yi >= 0) & (yi < H) & (xi >= 0) & (xi < W)).astype(xf.dtype)
                    idx = jnp.clip(yi, 0, H - 1) * W + jnp.clip(xi, 0, W - 1)
                    v = jnp.take(xf, idx.reshape(-1), axis=1).reshape(C, KK, Ho, Wo)
                    acc = acc + v * (wgt * valid)[None]
                return acc
            vals = jax.vmap(sample_one)(x.reshape(B, C, H * W), ys, xs)
            out = jnp.einsum('bckhw,ock->bohw', vals, w.reshape(w.shape[0], C, KK))
            return out + b[None, :, None, None]
        offset = conv2d(x, offset_w, offset_b)
        return deform_conv(x, offset, deform_w, deform_b)

    def _L3_conv_ref(x, w1, b1, w2, b2, w3, b3):
        import jax, jax.numpy as jnp
        import numpy as np
        B, C, H, W = (4, 32, 32, 32)
        Bb, Cc, Hh, Ww = x.shape
        N = Hh * Ww
        xf = x.reshape(Bb, Cc, N)
        f1 = jnp.einsum('oc,bcn->bon', w1, xf) + b1[None, :, None]
        f2 = jnp.einsum('oc,bcn->bon', w2, xf) + b2[None, :, None]
        f3 = jnp.einsum('oc,bcn->bon', w3, xf) + b3[None, :, None]
        A = jax.nn.softmax(jnp.einsum('bcn,bcm->bnm', f1, f2), axis=-1)
        out = jnp.einsum('bcm,bnm->bcn', f3, A) + xf
        return out.reshape(Bb, Cc, Hh, Ww)

    def _gn(v, G=32, eps=1e-05):
        B_, C_, H_, W_ = v.shape
        g = v.reshape(B_, G, C_ // G, H_, W_)
        m = jnp.mean(g, axis=(2, 3, 4), keepdims=True)
        s = jnp.var(g, axis=(2, 3, 4), keepdims=True)
        return ((g - m) / jnp.sqrt(s + eps)).reshape(v.shape)

    def _ln_c(v, eps=1e-06):
        m = jnp.mean(v, axis=1, keepdims=True)
        s = jnp.var(v, axis=1, keepdims=True)
        return (v - m) / jnp.sqrt(s + eps)

    def _ln_t(v, eps=1e-05):
        m = jnp.mean(v, axis=-1, keepdims=True)
        s = jnp.var(v, axis=-1, keepdims=True)
        return (v - m) / jnp.sqrt(s + eps)

    def _to_tokens(v):
        B_, C_, H_, W_ = v.shape
        return v.reshape(B_, C_, H_ * W_).transpose(0, 2, 1)

    def _from_tokens(t, like):
        B_, C_, H_, W_ = like.shape
        return t.transpose(0, 2, 1).reshape(B_, C_, H_, W_)
    x = x + _L0_conv_ref(_gn(x), L0_conv_conv_w, L0_conv_off_w, L0_conv_off_b, L0_conv_mask_w, L0_conv_mask_b, L0_conv_gamma, L0_conv_beta)
    x = x + _L1_conv_ref(_gn(x), L1_conv_weight, L1_conv_alpha_x, L1_conv_alpha_w)
    x = x + _L2_conv_ref(_gn(x), L2_conv_offset_w, L2_conv_offset_b, L2_conv_deform_w, L2_conv_deform_b)
    x = x + _L3_conv_ref(_gn(x), L3_conv_w1, L3_conv_b1, L3_conv_w2, L3_conv_b2, L3_conv_w3, L3_conv_b3)
    return x

_drawn_inputs = setup_inputs


def setup_inputs(seed=0):
    import zlib

    import numpy as np

    out = dict(_drawn_inputs(seed))
    spreads = {'L0_conv_gamma': (1.0, 0.2), 'L0_conv_beta': (0.0, 0.1), 'L2_conv_offset_b': (0.0, 0.692)}
    factors = {'L2_conv_deform_b': 58.572, 'L3_conv_b1': 38.768, 'L3_conv_b2': 64.0, 'L3_conv_b3': 55.006}
    for name, (base, spread) in spreads.items():
        noise = np.random.default_rng([zlib.crc32(name.encode()), seed]).standard_normal(out[name].shape)
        drawn = base * np.exp(spread * noise) if base else spread * noise
        out[name] = jnp.asarray(drawn.astype(out[name].dtype))
    for name, factor in factors.items():
        out[name] = (out[name] * factor).astype(out[name].dtype)
    return out
```

```python
import concourse.bass as bass
from concourse import mybir
from contextlib import ExitStack

F32 = mybir.dt.float32
BF16 = mybir.dt.bfloat16
I32 = mybir.dt.int32
U32 = mybir.dt.uint32
ALU = mybir.AluOpType
ACT = mybir.ActivationFunctionType
AXIS_X = mybir.AxisListType.X

B, C, H, W = 2, 32, 64, 64
N = H * W
TAPS = 9
P = 128
TILES = N // P
GRID = H + 1
PITCH = W + 2
QPIX = -(-GRID * PITCH // P) * P
QTILES = QPIX // P
BLK = 512
NBLK = N // BLK
CORNERS = 4
GROUPS = TILES // 4
WINDOW = 5
NEAR = 3
LEAD = 2 * PITCH + 4
TAIL = 4
OFFS = 3 * TAPS
EPS = 1e-5
QUADS_CLEARED = 8
POOL_CONSTS = QUADS_CLEARED + 12
DEFORMS = 2
SPLITS = 3
PAIRS = TILES // 2
KEY_PAIRS = TILES // 2
FIRST_MERGED = 4
MERGED = (PAIRS - FIRST_MERGED) // 2
CHUNKS = [2] * 8 + [3] * 4 + [2] * 2 + [0] * 2
MERGED_CHUNKS = [2, 2, 3, 3, 1, 2, 3, 3, 1, 2, 3, 3, 2, 2, 0, 0]
LAST_CHUNKS = [0] * 7 + [4] * 8 + [0]
SUM_AT = [1, 2, 3, 4, 5, 6, 7]
MERGED_SUM_AT = [2, 3, 6, 7, 10, 11, 14]
SCORES, SUMS, FREE, SAMPLES = 0, 4, 5, 7


def build(nc, x, off_w, off_b, conv_w, gamma, beta, l1_w, l1_ax, l1_aw, off2_w, off2_b, conv2_w, conv2_b,
          w123, b123, out):
    ctx = ExitStack()
    with ctx:
        def sb(name, shape, dt=F32):
            return ctx.enter_context(nc.sbuf_tensor(name, shape, dt))

        def sem(name):
            return ctx.enter_context(nc.semaphore(name))

        quad_table = [[nc.dram_tensor(f"quad_table_{d}_{b}", [QPIX, CORNERS * C], F32, kind="Internal").ap()
                       for b in range(B)] for d in range(DEFORMS)]

        padded = [nc.dram_tensor(f"padded_image_{b}", [LEAD + QPIX + TAIL, C], F32, kind="Internal").ap()
                  for b in range(B)]

        xs = sb("x_state", [C, B, N])
        y_all = sb("products_or_attention", [P, B * N])
        ys = y_all[0:C, :].rearrange("p (b n) -> p b n", b=B)
        far_corners = y_all[:, 2 * NEAR * NEAR * TAPS * C:][:, 0:2 * TAPS * CORNERS * C].rearrange(
            "p (u n) -> p u n", u=2)
        products = y_all[:, 0:2 * NEAR * NEAR * TAPS * C].rearrange("p (u n) -> p u n", u=2)
        att = y_all[:, :].bitcast(BF16).rearrange("p (s n) -> p s n", s=4)
        qa_0, ka_0, qb, kb = (att[:, s, :] for s in range(4))
        quads = sb("quads", [P, B, QPIX])
        arena = sb("quad_rows_or_splits", [P, SPLITS * N // 2])
        quad_rows = arena[:, 0:QTILES * P].rearrange("p (t e) -> p t e", t=QTILES)
        l1_normed_q, l1_tanh_q, l1_sign_q = (arena[:, N // 4 * k:N // 4 * (k + 1)] for k in range(3))
        windows = arena[:, QTILES * P:QTILES * P + 2 * WINDOW * WINDOW * C].rearrange(
            "p (u y e) -> p u y e", u=2, y=WINDOW)
        tail = QTILES * P + 2 * WINDOW * WINDOW * C
        near_w = arena[:, tail:tail + TAPS * NEAR * NEAR].rearrange("p (k d) -> p k d", k=TAPS)
        tail += TAPS * NEAR * NEAR
        conv_stats = arena[0:C, tail:tail + B * NBLK * 6]
        parts = arena[0:2 * C, :].bitcast(BF16).rearrange("p (s n) -> p s n", s=SPLITS)
        g2 = sb("conv_sums_or_normed", [2 * C, N])
        conv_sums = [g2[C * b:C * b + C, :] for b in range(B)]
        scratch = sb("scratch", [P, 4096])
        work = sb("probs_and_weighted", [P, 4 * BLK + CORNERS * TAPS * C])
        probs = work[:, 0:4 * BLK].rearrange("p (u n) -> p u n", u=2)
        weighted = work[:, 4 * BLK:4 * BLK + CORNERS * TAPS * C]
        tile_data = sb("tile_data", [P, 2 * TAPS * CORNERS * C + B * TILES * TAPS * CORNERS])
        gathered = tile_data[:, 0:2 * TAPS * CORNERS * C].rearrange("p (u n) -> p u n", u=2)
        corner_w = tile_data[:, 2 * TAPS * CORNERS * C:].rearrange("p (t k) -> p t k", t=B * TILES)
        late = tile_data[:, 0:N].bitcast(BF16).rearrange("p (s n) -> p s n", s=2)
        qa, ka = (qa_0, late[:, 0, :]), (ka_0, late[:, 1, :])
        hats = sb("hats", [P, B * GROUPS * 2, 2, TAPS, NEAR])
        reach = sb("reach", [P, 2 * B])
        in_reach = sb("in_reach", [1, B], U32)
        zeros = sb("zeros", [P, LEAD * C // P])
        sampled = sb("sampled", [P, 2, TAPS * C])
        vals = sb("vals", [3 * C, 2, 3 * P])
        index_f = sb("index_f", [P, B * TILES + 4, TAPS])
        index_u = sb("index_u", [P, 4, TAPS], U32)
        base = sb("base", [P, TILES, TAPS, 2])
        ident = sb("ident", [P, P])
        ident_h = sb("ident_h", [P, P], BF16)
        ones = sb("ones", [P, P])
        off_w_sb = [sb(f"off_w_{d}", [P, 4, C]) for d in range(DEFORMS)]
        off_b_row = sb("off_b_row", [1, DEFORMS, OFFS])
        off_b_all = sb("off_b_all", [P, DEFORMS, OFFS])
        conv_w_sb = [sb(f"conv_w_{d}", [3 * C, 3, C]) for d in range(DEFORMS)]
        col = sb("columns", [C, 3])
        alpha = sb("alpha", [P, 2])
        l1_sb = sb("l1_sb", [P, 2, C])
        l1_tmp = sb("l1_tmp", [C, 4, C])
        w123_sb = sb("w123_sb", [C + 1, 3 * C])
        stats = sb("stats", [C, B * NBLK, 6])
        eps = sb("eps", [C, 1])
        mv = sb("mv", [C, 16, 4])
        norm = sb("norm", [C, 16, 2])
        maxes = sb("maxes", [P, 4, NBLK])
        bn_affine = sb("bn_affine", [B * C, 2])
        one_more = sb("one_more", [C, B])
        neg_max = sb("neg_max", [P, 3, 4])
        nm_parts = sb("nm_parts", [P, 4, SPLITS], BF16)
        psum = ctx.enter_context(nc.psum_tensor("psum", [P, 8, BLK], F32))

        def part(n, width, dt=F32):
            a = scratch[:, n:n + width]
            return a if dt == F32 else a.bitcast(dt)
        CO = TILES * TAPS * 2
        offs = part(0, TILES * OFFS)
        flat_offs = part(864, 2 * BLK).rearrange("p (h n) -> p h n", h=2)
        pos = part(864, CO)
        floor_i = part(864 + CO, CO, I32)
        floor_f = part(864 + 2 * CO, CO)
        above = part(864 + 3 * CO, CO)
        frac = part(864 + 3 * CO, 2 * CO).rearrange("p (t k c w) -> p t k c w", t=TILES, k=TAPS, c=2)
        att_sum = scratch[0:2 * C, 0:4 * BLK].rearrange("p (s n) -> p s n", s=4)
        att_halves = scratch[:, 4 * BLK:5 * BLK]
        flat_quads = quads[:, :, :].rearrange("p b n -> p (b n)")
        values = TILES * 2 * C
        f3 = [flat_quads[:, at:at + values].rearrange("p (t c) -> p t c", t=TILES)
              for at in (0, B * QPIX - values)]
        g3 = (g2, flat_quads[0:2 * C, values:values + N])
        f3_flat = arena[2 * C:3 * C, 0:N]
        remainder = [scratch[0:2 * C, (5 + u) * BLK:(6 + u) * BLK] for u in range(2)]

        consts_loaded = sem("consts_loaded"); x_loaded = [sem(f"x_loaded_{b}") for b in range(B)]
        out_stored = sem("out_stored")
        pool_consts = sem("pool_consts"); ident_made = sem("ident_made"); bias_spread = sem("bias_spread")
        dve = sem("dve_chain")
        var_ready = sem("var_ready"); dev_ready = sem("dev_ready"); norm_ready = sem("norm_ready")
        quads_ready = sem("quads_ready"); convs = sem("convs_done"); convs_copied = sem("convs_copied")
        convs_turned = sem("convs_turned"); offs_ready = sem("offs_ready"); indexed = sem("indexed")
        rows_turned = sem("rows_turned"); rows_copied = sem("rows_copied")
        rows_stored = [[sem(f"rows_stored_{d}_{b}") for b in range(B)] for d in range(DEFORMS)]
        mask_ready = sem("mask_ready"); index_ready = sem("index_ready")
        padded_stored = [sem(f"padded_stored_{b}") for b in range(B)]
        window_loads = [sem(f"window_loads_{u}") for u in range(2)]
        far_gathers = [[sem(f"far_gathers_{b}_{u}") for u in range(2)] for b in range(B)]
        reach_ready = sem("reach_ready"); reach_turned = sem("reach_turned"); reach_known = sem("reach_known")
        affine_ready = sem("affine_ready"); conv_stat = sem("conv_stats_done")
        gathers = [sem(f"gathers_{u}") for u in range(2)]
        tile_steps = sem("tile_steps"); samples = sem("samples_ready"); turned = sem("samples_turned")
        vals_ready = sem("vals_ready"); outs = sem("outs_done"); outs_read = sem("outs_read")
        bn_out = sem("bn_out")
        l1_g = sem("l1_g"); l1_signs = sem("l1_signs"); l1_tanh = sem("l1_tanh"); l1_mm = sem("l1_mm")
        block_stat = sem("block_stats"); finished_stat = sem("finished_stats")
        l1w_tanh = sem("l1w_tanh"); l1w_ready = sem("l1w_ready")
        g3_ready = sem("g3_ready"); f_mm = sem("f_mm"); f_hi = sem("f_hi"); f_rem = sem("f_rem")
        f_parts = sem("f_parts"); spread_a = [sem(f"parts_spread_a_{b}") for b in range(B)]
        spread_b = [sem(f"parts_spread_b_{b}") for b in range(B)]
        f3_turned = sem("f3_turned"); f3_ready = sem("f3_ready")
        chunk_scored = sem("chunk_scored"); maxed = sem("maxed"); nm_steps = sem("nm_steps")
        nm_ready = sem("nm_ready"); nm_mm = sem("nm_mm"); nm_rows = sem("nm_rows")
        scored = sem("scores_ready"); probs_ready = sem("probs_ready"); summed = sem("sums_done")
        sums_copied = sem("sums_copied"); sum_steps = sem("sum_steps"); residuals = sem("residuals_added")
        x_final = sem("x_final")

        block = ctx.enter_context(nc.Block())
        SHIFTS = [(sy, sx, [(dy, dx) for dy in range(2) for dx in range(2)
                            if (dy == 1 or sy == 0) and (dx == 1 or sx == 0)]) for sy in range(2) for sx in range(2)]
        N_CONST = 16 * (9 * DEFORMS + 12)
        CHUNK_N = TILES // NBLK * NBLK
        NM_STEPS, SUM_STEPS = 5, 7

        def lin(n, scale=1, off=0):
            var, step, start = n
            if isinstance(var, int):
                return (var * step + start) * scale + off
            return var * (step * scale) + (start * scale + off)

        def wait(eng, semaphore, value):
            if not isinstance(value, int) or value > 0:
                eng.wait_ge(semaphore, value)

        def norm_at(stage, b):
            return [(0, 0), (0, 1), (0, B), (1, 0), (2, 0), (1, 1), (2, 1), (3, 0), (3, 1)].index((stage, b))

        def phase(d, b):
            return B * d + b

        def pair_of(i):
            return (i, 1, 0)

        def tile_no(d, b, pair, u):
            var, step, start = pair
            return (var, 2 * step, 2 * start + TILES * phase(d, b) + u)

        def window_tile(b, group, slot, u):
            var, step, start = group
            return (var, 4 * step, 4 * start + TILES * b + 2 * slot + u)

        VALUES_AT = [(NBLK - 1, s) for s in range(4, 8)]
        SPLIT_AT = [(NBLK - 2, s) for s in range(4, KEY_PAIRS, 2)] + [(NBLK - 1, 0), (NBLK - 1, 2)]

        def split_bank(b, j):
            return SAMPLES if b else SCORES + j % 4

        def values_bank(b, h):
            return SAMPLES if b else FREE + h % 2

        def sample_bank(d, u):
            return SCORES + 2 + u if d == 0 else SAMPLES

        def rows_at(value, size=1):
            return slice(value, value + size) if isinstance(value, int) else bass.ds(value, size)

        def merged_pair(j, t):
            var, step, start = j
            return (var, 2 * step, 2 * start + FIRST_MERGED + t // 2), t % 2

        def quad_write(op, q, d, b, on_scalar=False):
            dy, dx = q // 2, q % 2
            dst = quads[C * q:C * q + C, b, 0:GRID * PITCH].rearrange("p (y x) -> p y x", x=PITCH)
            dst = dst[:, 1 - dy:1 - dy + H, 1 - dx:1 - dx + W]
            src = xs[:, b, :].rearrange("p (y x) -> p y x", x=W)
            n = norm_at(2 * d, b)
            if on_scalar:
                return op(dst, src, ACT.Identity, scale=norm[:, n, 0:1], bias=norm[:, n, 1:2])
            return op(dst, src, norm[:, n, 0:1], norm[:, n, 1:2], ALU.mult, ALU.add)

        @block.sync
        def _(sp):
            for b in range(B):
                sp.dma_start(xs[:, b, :], x[b].rearrange("c h w -> c (h w)")).then_inc(x_loaded[b], 16)
            sp.wait_ge(pool_consts, 3)
            for d, w in enumerate((off_w, off2_w)):
                for s, (sy, sx, cover) in enumerate(SHIFTS):
                    for dy, dx in cover:
                        q = 2 * dy + dx
                        sp.dma_start(off_w_sb[d][C * q:C * q + C, s, 0:OFFS - TAPS * d],
                                     w[sy + dy, sx + dx]).then_inc(consts_loaded, 16)
            sp.dma_start(off_b_row[:, 0, :], off_b).then_inc(consts_loaded, 16)
            sp.dma_start(off_b_row[:, 1, 0:2 * TAPS], off2_b).then_inc(consts_loaded, 16)
            for d, w in enumerate((conv_w, conv2_w)):
                sp.dma_start(conv_w_sb[d][:, :, :], w.rearrange("g p o -> p g o")).then_inc(consts_loaded, 16)
            for j, v in enumerate((gamma, beta, conv2_b)):
                sp.dma_start(col[:, j:j + 1], v).then_inc(consts_loaded, 16)
            for j, v in enumerate((l1_ax, l1_aw)):
                sp.dma_start(alpha[:, j:j + 1], v.to_broadcast([P, 1])).then_inc(consts_loaded, 16)
            sp.dma_start(l1_tmp[:, 0, :], l1_w).then_inc(consts_loaded, 16)
            sp.dma_start(w123_sb[0:C, :], w123).then_inc(consts_loaded, 16)
            sp.dma_start(w123_sb[C:C + 1, :], b123).then_inc(consts_loaded, 16)

            for b in range(B):
                sp.dma_start(padded[b][0:LEAD, :].rearrange("r c -> (r c)").rearrange("(p n) -> p n", p=P),
                             zeros[:, :]).then_inc(padded_stored[b], 16)
                sp.dma_start(padded[b][LEAD + QPIX:LEAD + QPIX + TAIL, :].rearrange("r c -> (r c)")
                             .rearrange("(p n) -> p n", p=P), zeros[:, 0:1]).then_inc(padded_stored[b], 16)
            for d in range(DEFORMS):
                for b in range(B):
                    for g0, g1 in ((0, 3), (3, 6), (6, 9)):
                        t0, t1 = 4 * g0, min(4 * g1, QTILES)
                        sp.wait_ge(rows_copied, 9 * phase(d, b) + g1)
                        sp.dma_start(quad_table[d][b].rearrange("(t p) e -> p t e", p=P)[:, t0:t1, :],
                                     quad_rows[:, t0:t1, :]).then_inc(rows_stored[d][b], 16)
                        if d == 0:
                            sp.dma_start(padded[b][LEAD + P * t0:LEAD + P * t1, :].rearrange("(t p) c -> p t c", p=P),
                                         quad_rows[:, t0:t1, 3 * C:4 * C]).then_inc(padded_stored[b], 16)
            for b in range(B):
                sp.wait_ge(f_parts, b + 1)
                hi, mid, lo = (parts[:, s, :] for s in range(SPLITS))
                for dst, first, srcs in ((qa[b], 0, (hi, hi, mid, mid)), (ka[b], C, (hi, mid, hi, mid))):
                    for at, src in enumerate(srcs):
                        sp.dma_start(dst[C * at:C * at + C, :], src[first:first + C, :]).then_inc(spread_a[b], 16)
                if b:
                    sp.wait_ge(scored, KEY_PAIRS * NBLK * b)
                for dst, first, srcs in ((qb, 0, (hi, lo)), (kb, C, (lo, hi))):
                    for at, src in enumerate(srcs):
                        sp.dma_start(dst[C * at:C * at + C, :], src[first:first + C, :]).then_inc(spread_b[b], 16)
            for b in range(B):
                sp.wait_ge(x_final, NBLK * (b + 1))
                sp.dma_start(out[b].rearrange("c h w -> c (h w)"), xs[:, b, :]).then_inc(out_stored, 16)
            sp.wait_ge(out_stored, 16 * B)

        @block.gpsimd
        def _(pool):
            made = [0]

            def const(ins):
                made[0] += 1
                ins.then_inc(pool_consts, 1)
                pool.wait_ge(pool_consts, made[0])

            for d in range(DEFORMS):
                const(pool.memset(off_w_sb[d][:, :, :], 0.0))
            const(pool.memset(zeros[:, :], 0.0))
            const(pool.memset(eps[:, :], EPS))
            const(pool.memset(ident[:, :], 0.0))
            pool.affine_select(out=ident[:, :], in_=ident[:, :], compare_op=ALU.not_equal, fill=1.0, base=0,
                               pattern=[[-1, P]], channel_multiplier=1).then_inc(ident_made, 1)
            pool.wait_ge(ident_made, 1)
            pool.tensor_copy(ident_h[:, :], ident[:, :]).then_inc(ident_made, 1)
            pool.wait_ge(ident_made, 2)
            const(pool.memset(ones[:, :], 1.0))
            const(pool.memset(index_f[:, :, :], 0.0))
            const(pool.memset(quads[:, 0, :], 0.0))
            assert made[0] == QUADS_CLEARED
            for h in range(2):
                rows = slice(64 * h, 64 * h + 64)
                for ky in range(3):
                    const(pool.iota(base[rows, :, 3 * ky:3 * ky + 3, 0], [[2, TILES], [0, 3]], base=h + ky,
                                    channel_multiplier=0, allow_small_or_imprecise_dtypes=True))
                    const(pool.iota(base[rows, :, 3 * ky:3 * ky + 3, 1], [[0, TILES], [1, 3]], base=0,
                                    channel_multiplier=1, allow_small_or_imprecise_dtypes=True))
            assert made[0] == POOL_CONSTS

            for d in range(DEFORMS):
                pool.wait_ge(norm_ready, norm_at(2 * d, 0) + 1)
                quad_write(pool.tensor_scalar, 3, d, 0).then_inc(quads_ready, 1)
                if d == 0:
                    pool.wait_ge(quads_ready, 4)
                    const(pool.memset(quads[:, 1, :], 0.0))

                def gather(b, out, rows, done):
                    for k in range(TAPS):
                        pool.indirect_dma_start(
                            out=out[:, k * CORNERS * C:(k + 1) * CORNERS * C], out_offset=None,
                            in_=quad_table[d][b],
                            in_offset=bass.IndirectOffsetOnAxis(ap=index_u[:, rows, k:k + 1], axis=0),
                        ).then_inc(done, 16)

                def await_samples(n):
                    pool.wait_ge(samples, lin(n, 1, 1))
                    pool.nop(nofuse=True)

                def group(b, g, near, first=False):
                    var, step, start = g
                    for u in range(2):
                        if not first:
                            await_samples(window_tile(b, (var, step, start - 1), 1, u))
                            gather(b, gathered[:, u, :], u, gathers[u])
                    with pool.If(near == 0):
                        for u in range(2):
                            gather(b, far_corners[:, u, :], 2 + u, far_gathers[b][u])

                for b in range(B):
                    pool.wait_ge(rows_stored[d][b], 48)
                    if b == 0:
                        pool.wait_ge(index_ready, d + 1)
                        for u in range(2):
                            gather(b, gathered[:, u, :], u, gathers[u])
                    if d == 0:
                        pool.wait_ge(reach_known, b + 1)
                        near = pool.value_load(in_reach[0:1, b:b + 1], min_val=0, max_val=1)
                        group(b, (0, 0, 0), near, first=b == 0)
                        with pool.Fori(1, GROUPS) as i:
                            group(b, (i, 1, 0), near)
                    else:
                        with pool.Fori(1 if b == 0 else 0, PAIRS) as i:
                            for u in range(2):
                                await_samples((i, 2, TILES * phase(d, b) + u - 2))
                                gather(b, gathered[:, u, :], u, gathers[u])

        @block.vector
        def _(v):
            count, block_count = [0], [0]

            def step(ins):
                count[0] += 1
                ins.then_inc(dve, 1)
                v.wait_ge(dve, count[0])

            def normalise(n, tensor, gammas=None, known=None):
                for j, piece in enumerate(tensor):
                    last = v.bn_stats(stats[:, j, :], piece)
                if known is None:
                    step(last)
                    known = stats[:, 0:len(tensor), :]
                v.bn_aggr(mv[:, n, 0:2], known).then_inc(var_ready, 1)
                v.wait_ge(dev_ready, n + 1)
                if gammas is None:
                    step(v.reciprocal(norm[:, n, 0:1], mv[:, n, 2:3]))
                    v.scalar_tensor_tensor(norm[:, n, 1:2], mv[:, n, 0:1], -1.0, norm[:, n, 0:1],
                                           ALU.mult, ALU.mult).then_inc(norm_ready, 1)
                else:
                    step(v.reciprocal(mv[:, n, 3:4], mv[:, n, 2:3]))
                    step(v.tensor_tensor(norm[:, n, 0:1], mv[:, n, 3:4], gammas[0], ALU.mult))
                    step(v.scalar_tensor_tensor(norm[:, n, 1:2], mv[:, n, 0:1], -1.0, norm[:, n, 0:1],
                                                ALU.mult, ALU.mult))
                    v.tensor_tensor(norm[:, n, 1:2], norm[:, n, 1:2], gammas[1], ALU.add).then_inc(norm_ready, 1)
                v.wait_ge(norm_ready, n + 1)

            def pieces(t, b):
                return [t[:, b, BLK * j:BLK * j + BLK] for j in range(NBLK)]

            def two_quads(d, b):
                if d:
                    normalise(norm_at(2, b), [], None, stats_of_blocks())
                for q in range(2):
                    quad_write(v.tensor_scalar, q, d, b).then_inc(quads_ready, 1)

            def offsets_of(d):
                width = OFFS - TAPS * d
                return offs[:, 0:TILES * width].rearrange("p (t c) -> p t c", c=width), width

            def corners(d, b):
                o, width = offsets_of(d)
                for h in range(2):
                    v.wait_ge(convs_turned, 2 * phase(d, b) + h + 1)
                    for g in range(4):
                        t = 16 * h + 4 * g
                        last = v.tensor_tensor(
                            o[:, t:t + 4, :],
                            psum[:, FREE + h, :].rearrange("p (t g c) -> p g t c", g=4, c=C)[:, g, :, 0:width],
                            off_b_all[:, d, None, 0:width].to_broadcast([P, 4, width]), ALU.add)
                last.then_inc(offs_ready, 1)
                v.wait_ge(offs_ready, phase(d, b) + 1)
                p4 = pos.rearrange("p (t k) -> p t k", t=TILES)
                step(v.tensor_tensor(p4, o[:, :, 0:2 * TAPS], base[:, :, :, :].rearrange("p t k c -> p t (k c)"),
                                     ALU.add))
                step(v.tensor_scalar(pos, pos, 0.0, float(H + 1), ALU.max, ALU.min))
                step(v.tensor_copy(floor_i, pos))
                step(v.tensor_copy(floor_f, floor_i))
                step(v.tensor_tensor(above, floor_f, pos, ALU.is_gt))
                step(v.tensor_tensor(floor_f, floor_f, above, ALU.subtract))
                step(v.tensor_scalar(floor_f, floor_f, float(H), None, ALU.min))

            def indices(d, b):
                o, width = offsets_of(d)
                fr = frac[:, :, :, :, :].rearrange("p t k c w -> p (t k c) w")
                step(v.tensor_tensor(fr[:, :, 1], pos, floor_f, ALU.subtract))
                step(v.tensor_scalar(fr[:, :, 0], fr[:, :, 1], -1.0, 1.0, ALU.mult, ALU.add))
                tk = frac[:, :, :, :, :].rearrange("p t k c w -> p (t k) c w")
                if d == 0:
                    v.wait_ge(mask_ready, b + 1)
                    step(v.tensor_tensor(frac[:, :, :, 0, :], frac[:, :, :, 0, :],
                                         o[:, :, 2 * TAPS:, None].to_broadcast([P, TILES, TAPS, 2]), ALU.mult))
                mine = slice(TILES * b, TILES * b + TILES)
                cw = corner_w[:, mine, :].rearrange("p t (k y x) -> p (t k) y x", k=TAPS, y=2)
                for dx in range(2):
                    v.tensor_tensor(cw[:, :, :, dx], tk[:, :, 0, :],
                                    tk[:, :, 1, dx:dx + 1].to_broadcast([P, TILES * TAPS, 2]),
                                    ALU.mult)
                ff = floor_f.rearrange("p (t k c) -> p t k c", t=TILES, c=2)
                v.scalar_tensor_tensor(index_f[:, mine, :], ff[:, :, :, 0], float(PITCH), ff[:, :, :, 1],
                                       ALU.mult, ALU.add).then_inc(indexed, 1)
                v.wait_ge(indexed, phase(d, b) + 1)
                if (d, b) == (0, 0):
                    v.tensor_copy(index_u[:, 2:4, :], index_f[:, 0:2, :])
                    v.tensor_copy(index_u[:, 0:2, :], index_f[:, 2:4, :]).then_inc(index_ready, 1)
                if (d, b) == (1, 0):
                    v.tensor_copy(index_u[:, 0:2, :], index_f[:, 0:2, :]).then_inc(index_ready, 1)

            def hat_weights(b):
                delta = part(864 + CO, CO)
                step(v.tensor_tensor(delta, pos, base[:, :, :, :].rearrange("p t k c -> p (t k c)"), ALU.subtract))
                mine = hats[:, 2 * GROUPS * b:2 * GROUPS * (b + 1)]
                by_tile = mine.rearrange("p (g f) c k j -> p g f (c k) j", f=2)
                for f in range(2):
                    for c in range(2):
                        src = delta.rearrange("p (g f k c) -> p g f k c", g=GROUPS, f=4, c=2)[:, :, f, :, c]
                        v.tensor_scalar(by_tile[:, :, f, TAPS * c:TAPS * c + TAPS, 0], src, -1.0, 0.0, ALU.mult, ALU.max)
                        last = v.tensor_scalar(by_tile[:, :, f, TAPS * c:TAPS * c + TAPS, 2], src, 0.0, None, ALU.max)
                step(last)
                flat = mine.rearrange("p t c k j -> p j (t c k)")
                step(v.tensor_tensor(flat[:, 1, :], flat[:, 0, :], flat[:, 2, :], ALU.add))
                v.reduce_max(reach[:, b:b + 1], flat[:, 1, :], AXIS_X).then_inc(reach_ready, 1)
                v.wait_ge(reach_ready, b + 1)
                step(v.tensor_scalar(flat[:, 1, :], flat[:, 1, :], -1.0, 1.0, ALU.mult, ALU.add))
                o, _ = offsets_of(0)
                m = o.rearrange("p (g f) c -> p g f c", f=4)
                for f in range(2):
                    rows_w = by_tile[:, :, f, 0:TAPS, :]
                    last = v.tensor_tensor(rows_w, rows_w, m[:, :, f, 2 * TAPS:, None]
                                           .to_broadcast([P, GROUPS, TAPS, NEAR]), ALU.mult)
                step(last)
                v.wait_ge(reach_turned, b + 1)
                step(v.reduce_max(reach[0:1, 2 + b:3 + b], psum[0:1, FREE, 0:P], AXIS_X))
                v.tensor_scalar(in_reach[:, b:b + 1], reach[0:1, 2 + b:3 + b], 1.0, None, ALU.is_lt)\
                    .then_inc(reach_known, 1)
                v.wait_ge(reach_known, b + 1)

            def corner_products(n, cols, corners_of):
                wait(v, samples, lin(n))
                v.tensor_tensor(
                    weighted[:, :].rearrange("p (q k c) -> p k q c", q=CORNERS, c=C),
                    corners_of.rearrange("p (k q c) -> p k q c", k=TAPS, q=CORNERS),
                    corner_w[:, rows_at(cols), :].rearrange("p a (k q) -> p (a k) q", q=CORNERS)
                    [:, :, :, None].to_broadcast([P, TAPS, CORNERS, C]), ALU.mult).then_inc(tile_steps, 1)

            def corner_sums(n, u):
                v.wait_ge(tile_steps, lin(n, 2, 1))
                half = 2 * TAPS * C
                v.tensor_tensor(weighted[:, 0:half], weighted[:, 0:half], weighted[:, half:2 * half], ALU.add)\
                    .then_inc(tile_steps, 1)
                v.wait_ge(tile_steps, lin(n, 2, 2))
                wait(v, turned, lin(n, 1, -1))
                v.tensor_tensor(sampled[:, u, :], weighted[:, 0:half // 2], weighted[:, half // 2:half], ALU.add)\
                    .then_inc(samples, 1)

            def weight_corners(d, b, pair, u):
                var, stp, start = pair
                v.wait_ge(gathers[u], lin((var, stp, start + GROUPS * B + PAIRS * b), 16 * TAPS, 16 * TAPS))
                own = lin((var, 2 * stp, 2 * start + TILES * b + u))
                v.tensor_copy(index_u[:, u, :], index_f[:, rows_at(own + 2), :].rearrange("p a k -> p (a k)"))
                corner_products(tile_no(d, b, pair, u), own, gathered[:, u, :])

            def sum_corners(d, b, pair, u):
                corner_sums(tile_no(d, b, pair, u), u)

            def gathered_tile(b, group, u):
                n = window_tile(b, group, 1, u)
                var, stp, start = group
                v.wait_ge(gathers[u], lin((var, stp, start + GROUPS * b), 16 * TAPS, 16 * TAPS))
                for rows, ahead in ((u, 4), (2 + u, 2)):
                    v.tensor_copy(index_u[:, rows, :],
                                  index_f[:, rows_at(lin(n, 1, ahead)), :].rearrange("p a k -> p (a k)"))
                corner_products(n, lin(n), gathered[:, u, :])
                corner_sums(n, u)

            def windowed_tile(b, group, u, near):
                n = window_tile(b, group, 0, u)
                var, stp, start = group
                v.wait_ge(window_loads[u], lin((var, stp, start + GROUPS * b), 32, 32))
                v.nop(nofuse=True)
                with v.If(near == 1):
                    h = hats[:, rows_at(lin((var, 2 * stp, 2 * start + 2 * GROUPS * b + u))), :, :, :]\
                        .rearrange("p t c k j -> p (t c) k j")
                    wait(v, samples, lin(n))
                    v.tensor_tensor(near_w[:, :, :].rearrange("p k (y x) -> p k y x", y=NEAR),
                                    h[:, 0, :, :, None].to_broadcast([P, TAPS, NEAR, NEAR]),
                                    h[:, 1, :, None, :].to_broadcast([P, TAPS, NEAR, NEAR]), ALU.mult)\
                        .then_inc(tile_steps, 1)
                    v.wait_ge(tile_steps, lin(n, 2, 1))
                    wait(v, turned, lin(n, 1, -1))
                    win = windows[:, u, :, :].rearrange("p y (x c) -> p y x c", c=C)
                    mine = products[:, u, :]
                    out9 = mine.rearrange("p (d ky kx c) -> p d ky kx c", d=NEAR * NEAR, ky=3, c=C)
                    w9 = near_w[:, :, :].rearrange("p (ky kx) d -> p d ky kx", ky=3)
                    for dy in range(NEAR):
                        for dx in range(NEAR):
                            d9 = NEAR * dy + dx
                            last = v.tensor_tensor(out9[:, d9], win[:, dy:dy + 3, dx:dx + 3, :],
                                                   w9[:, d9, :, :, None].to_broadcast([P, 3, 3, C]), ALU.mult)
                    last.then_inc(tile_steps, 1)
                    v.wait_ge(tile_steps, lin(n, 2, 2))
                    half = 4 * TAPS * C
                    v.tensor_tensor(mine[:, 0:half], mine[:, 0:half], mine[:, half:2 * half], ALU.add)\
                        .then_inc(samples, 1)
                with v.If(near == 0):
                    v.wait_ge(far_gathers[b][u], lin(group, 16 * TAPS, 16 * TAPS))
                    corner_products(n, lin(n), far_corners[:, u, :])
                    v.wait_ge(tile_steps, lin(n, 2, 1))
                    wait(v, turned, lin(n, 1, -1))
                    quarter = TAPS * C
                    v.tensor_copy(products[:, u, 0:CORNERS * quarter], weighted[:, :]).then_inc(tile_steps, 1)
                    v.memset(products[:, u, 2 * CORNERS * quarter:], 0.0).then_inc(samples, 1)

            def finish(b, pair, u):
                v.wait_ge(outs, lin(tile_no(1, b, pair, u), 1, 1))
                var, stp, start = pair
                at = lin((var, 2 * stp, 2 * start + u), P)
                here = slice(at, at + P) if isinstance(at, int) else bass.ds(at, P)
                v.scalar_tensor_tensor(xs[:, b, here], psum[0:C, SAMPLES, 3 * P:4 * P], col[:, 2:3], xs[:, b, here],
                                       ALU.add, ALU.add).then_inc(outs_read, 1)

            def finished_block_stats(b, j):
                var, stp, start = j
                v.wait_ge(outs_read, lin((var, stp, start + NBLK * phase(1, b)), 4, 4))
                kept = stats[:, :, :].rearrange("p j k -> p (j k)") if b else conv_stats
                v.bn_stats(kept[:, rows_at(lin(j, 6), 6)], xs[:, b, rows_at(lin(j, BLK), BLK)])\
                    .then_inc(finished_stat, 1)

            def do_pair(d, b, pair, jobs=()):
                for u in range(2):
                    weight_corners(d, b, pair, u)
                    sum_corners(d, b, pair, u)
                finish(b, pair, 0)
                for job in jobs:
                    job()
                finish(b, pair, 1)

            def conv_block_stats(b, j):
                var, stp, start = j
                v.wait_ge(outs_read, lin((var, stp, start + NBLK * b), 4, 4))
                v.bn_stats(conv_stats[:, rows_at(lin((var, stp, start + NBLK * b), 6), 6)],
                           conv_sums[b][:, rows_at(lin(j, BLK), BLK)]).then_inc(conv_stat, 1)

            def grouped_pairs(b, beside):
                near = v.value_load(in_reach[0:1, b:b + 1], min_val=0, max_val=1)
                for i in range(len(beside)):
                    for u in range(2):
                        if i % 2:
                            gathered_tile(b, (0, 0, i // 2), u)
                        else:
                            windowed_tile(b, (0, 0, i // 2), u, near)
                    for job in beside[i]:
                        job()
                with v.Fori(len(beside) // 2, GROUPS) as i:
                    for u in range(2):
                        windowed_tile(b, (i, 1, 0), u, near)
                    for u in range(2):
                        gathered_tile(b, (i, 1, 0), u)
                    if b:
                        conv_block_stats(0, (i, 1, 0))
                        conv_block_stats(1, (i, 1, -1))

            def pairs(d, b, beside):
                for i in range(len(beside)):
                    do_pair(d, b, pair_of(i), beside[i])
                    if i % 2:
                        finished_block_stats(b, (0, 0, i // 2))
                if b == 0:
                    with v.Fori(len(beside) // 2, PAIRS // 2) as i:
                        do_pair(d, b, (i, 2, 0))
                        do_pair(d, b, (i, 2, 1))
                        finished_block_stats(b, (i, 1, 0))

            def block_stats(b, j):
                v.bn_stats(stats[:, j, :], xs[:, b, BLK * j:BLK * j + BLK]).then_inc(block_stat, 1)
                block_count[0] += 1

            def stats_of_blocks():
                v.wait_ge(block_stat, block_count[0])
                return stats[:, 0:NBLK, :]

            def add_relu(b):
                v.wait_ge(bn_out, 5)
                step(v.tensor_tensor(xs[:, b, :], xs[:, b, :], ys[:, b, :], ALU.add))

            def l1_normed(b):
                n = norm_at(1, b)
                if b == 0:
                    normalise(n, [], None, stats_of_blocks())
                else:
                    normalise(n, pieces(xs, b))
                v.wait_ge(rows_stored[b][1 - b], 48)
                v.wait_ge(padded_stored[1], 80)
                for q in range(4):
                    last = v.tensor_scalar(l1_normed_q[C * q:C * q + C, :], xs[:, b, N // 4 * q:N // 4 * (q + 1)],
                                           norm[:, n, 0:1], norm[:, n, 1:2], ALU.mult, ALU.add)
                last.then_inc(l1_g, 1)

            def l1_sign_ste(b):
                v.wait_ge(l1_tanh, b + 1)
                step(v.tensor_tensor(l1_sign_q, l1_sign_q, l1_tanh_q, ALU.subtract))
                v.tensor_tensor(l1_sign_q, l1_sign_q, l1_tanh_q, ALU.add).then_inc(l1_signs, 1)

            def l1_add_out(b):
                for h in range(2):
                    v.wait_ge(l1_mm, 2 * b + h + 1)
                    for q in range(4):
                        j = 2 * q + h
                        here = slice(BLK * j, BLK * j + BLK)
                        step(v.tensor_tensor(xs[:, b, here], xs[:, b, here], psum[C * q:C * q + C, FREE + h, :],
                                             ALU.add))
                        block_stats(b, j)

            def l3_normed():
                v.memset(g3[0][C:C + 1, :], 1.0)
                v.memset(f3[0][:, :, C:2 * C], 1.0)
                v.memset(kb[2 * C:2 * C + SPLITS, :], 1.0)
                n = norm_at(3, 0)
                v.wait_ge(finished_stat, NBLK)
                normalise(n, [], None, conv_stats[:, 0:NBLK * 6].rearrange("p (j k) -> p j k", k=6))
                v.tensor_scalar(one_more[:, 0:1], norm[:, n, 0:1], 1.0, None, ALU.add)
                v.tensor_scalar(g3[0][0:C, :], xs[:, 0, :], norm[:, n, 0:1], norm[:, n, 1:2], ALU.mult, ALU.add)\
                    .then_inc(g3_ready, 1)

            def split(b, j):
                here = slice(BLK * j, BLK * j + BLK)
                hi, mid, lo = (parts[:, s, here] for s in range(SPLITS))
                rem = remainder[j % 2]
                v.wait_ge(f_hi, NBLK * b + j + 1)
                v.tensor_tensor(rem, psum[0:2 * C, split_bank(b, j), :], hi, ALU.subtract).then_inc(f_rem, 1)
                v.wait_ge(f_rem, NBLK * b + j + 1)
                step(v.tensor_copy(mid, rem))
                last = v.tensor_tensor(lo, rem, mid, ALU.subtract)
                if j == NBLK - 1:
                    last.then_inc(f_parts, 1)
                    v.wait_ge(f_parts, b + 1)
                else:
                    step(last)

            def take_values(b, h):
                v.wait_ge(f3_turned, 4 * b + h + 1)
                v.tensor_copy(f3[b][:, 8 * h:8 * h + 8, 0:C],
                              psum[:, values_bank(b, h), 0:8 * C].rearrange("p (t c) -> p t c", t=8))\
                    .then_inc(f3_ready, 1)

            def l3_split():
                for j in range(NBLK):
                    split(0, j)
                for h in range(4):
                    take_values(0, h)

            def prepare_image_1(j, s):
                n = norm_at(3, 1)
                if (j, s) == (NBLK - 2, 0):
                    step(v.memset(g3[1][C:C + 1, :], 1.0))
                    step(v.memset(f3[1][:, :, C:2 * C], 1.0))
                    v.wait_ge(finished_stat, 2 * NBLK)
                    v.bn_aggr(mv[:, n, 0:2], stats[:, 0:NBLK, :]).then_inc(var_ready, 1)
                if (j, s) == (NBLK - 2, 2):
                    v.wait_ge(dev_ready, n + 1)
                    step(v.reciprocal(norm[:, n, 0:1], mv[:, n, 2:3]))
                    step(v.tensor_scalar(one_more[:, 1:2], norm[:, n, 0:1], 1.0, None, ALU.add))
                    v.scalar_tensor_tensor(norm[:, n, 1:2], mv[:, n, 0:1], -1.0, norm[:, n, 0:1],
                                           ALU.mult, ALU.mult).then_inc(norm_ready, 1)
                    v.wait_ge(norm_ready, n + 1)
                if (j, s - 1) in SPLIT_AT:
                    split(1, SPLIT_AT.index((j, s - 1)))

            def take_image_1(j, s):
                if (j, s - 1) in VALUES_AT:
                    take_values(1, VALUES_AT.index((j, s - 1)))

            def queries(b, j, off=0):
                var, stp, start = j
                return (var, stp, start + NBLK * b + off)

            def largest(b, j, chunks):
                for c in chunks:
                    v.wait_ge(chunk_scored, lin(queries(b, j), CHUNK_N, c + 1))
                    v.reduce_max(maxes[:, c // NBLK, c % NBLK:c % NBLK + 1], psum[:, FREE + c % 2, :], AXIS_X)\
                        .then_inc(maxed, 1)

            def negated(b, j):
                q = queries(b, j)
                v.wait_ge(maxed, lin(q, CHUNK_N, CHUNK_N))
                ops = [lambda: v.reduce_max(neg_max[:, 0, :], maxes[:, :, :], AXIS_X),
                       lambda: v.tensor_scalar(neg_max[:, 1, :], neg_max[:, 0, :], -1.0, None, ALU.mult),
                       lambda: v.tensor_copy(nm_parts[:, :, 0], neg_max[:, 1, :]),
                       lambda: v.tensor_tensor(neg_max[:, 2, :], neg_max[:, 1, :], nm_parts[:, :, 0], ALU.subtract),
                       lambda: v.tensor_copy(nm_parts[:, :, 1], neg_max[:, 2, :])]
                assert len(ops) == NM_STEPS
                for k, op in enumerate(ops):
                    op().then_inc(nm_steps, 1)
                    v.wait_ge(nm_steps, lin(q, NM_STEPS, k + 1))
                v.tensor_tensor(nm_parts[:, :, 2], neg_max[:, 2, :], nm_parts[:, :, 1], ALU.subtract)\
                    .then_inc(nm_ready, 1)

            def maxima_row(b, j):
                v.wait_ge(nm_mm, lin(queries(b, j), 1, 1))
                at = lin(j, BLK)
                here = slice(at, at + BLK) if isinstance(at, int) else bass.ds(at, BLK)
                v.tensor_copy(qb[2 * C:2 * C + SPLITS, here], psum[2 * C:2 * C + SPLITS, FREE, :]).then_inc(nm_rows, 1)

            def sum_part(b, j, k):
                q = queries(b, j)
                total, inverse, quotient = att_sum[:, 1, :], att_sum[0:C, 2, :], att_sum[0:C, 3, :]
                if k == 0:
                    v.wait_ge(sums_copied, lin(q, 1, 1))
                    v.tensor_copy(att_sum[:, 0, :], att_halves[2 * C:4 * C, :]).then_inc(sum_steps, 1)
                    v.wait_ge(sum_steps, lin(q, SUM_STEPS, 1))
                    v.tensor_tensor(total, att_halves[0:2 * C, :], att_sum[:, 0, :], ALU.add).then_inc(sum_steps, 1)
                    v.wait_ge(sum_steps, lin(q, SUM_STEPS, 2))
                elif k <= 4:
                    part_of = slice(P * (k - 1), P * k)
                    v.reciprocal(inverse[:, part_of], att_sum[C:2 * C, 1, part_of]).then_inc(sum_steps, 1)
                elif k == 5:
                    v.wait_ge(sum_steps, lin(q, SUM_STEPS, 6))
                    v.tensor_tensor(quotient, total[0:C, :], inverse, ALU.mult).then_inc(sum_steps, 1)
                else:
                    v.wait_ge(sum_steps, lin(q, SUM_STEPS, 7))
                    at = lin(j, BLK)
                    here = slice(at, at + BLK) if isinstance(at, int) else bass.ds(at, BLK)
                    v.tensor_tensor(xs[:, b, here], xs[:, b, here], quotient, ALU.add).then_inc(x_final, 1)

            def attend(b, j, first=False, last=False, tiles=False, prepare=None):
                var, stp, start = j
                nxt, prev = (var, stp, start + 1), (var, stp, start - 1)
                c = 0
                if last and b == 0:
                    b_next, nxt, chunks = 1, (0, 0, 0), LAST_CHUNKS
                elif last:
                    b_next, chunks = b, [0] * KEY_PAIRS
                else:
                    b_next, chunks = b, MERGED_CHUNKS if tiles else CHUNKS
                more = sum(chunks) > 0
                for s in range(KEY_PAIRS):
                    if prepare is not None:
                        take_image_1(j[2], s)
                    largest(b_next, nxt, range(c, c + chunks[s]))
                    c += chunks[s]
                    if s in (MERGED_SUM_AT if tiles else SUM_AT) and not first:
                        sum_part(b, prev, (MERGED_SUM_AT if tiles else SUM_AT).index(s))
                    if tiles and s % 4 == 0 and s:
                        finish(1, *merged_pair(j, s // 4 - 1))
                    if tiles and s % 4 == 0:
                        weight_corners(1, 1, *merged_pair(j, s // 4))
                    if tiles and s % 4 == 1:
                        sum_corners(1, 1, *merged_pair(j, s // 4))
                    if prepare is not None:
                        prepare(s)
                    if s == KEY_PAIRS - (1 if last else 2) and more:
                        negated(b_next, nxt)
                    if s == KEY_PAIRS - 1 and more:
                        maxima_row(b_next, nxt)
                    if tiles and s == KEY_PAIRS - 1:
                        finish(1, *merged_pair(j, 3))
                        finished_block_stats(1, (var, stp, start + FIRST_MERGED // 2))

            def attention(b):
                joint = MERGED if b == 0 else 0
                v.wait_ge(residuals, 1 + 4 * b)
                attend(b, (0, 0, 0), first=True, tiles=joint > 0)
                if joint:
                    with v.Fori(1, joint) as j:
                        attend(b, (j, 1, 0), tiles=True)
                if b == 0:
                    assert joint == NBLK - 2
                    for j in range(joint, NBLK):
                        attend(b, (0, 0, j), last=j == NBLK - 1,
                               prepare=lambda s, j=j: prepare_image_1(j, s))
                else:
                    with v.Fori(1, NBLK - 1) as j:
                        attend(b, (j, 1, 0))
                    attend(b, (0, 0, NBLK - 1), last=True)
                for k in range(len(SUM_AT)):
                    sum_part(b, (0, 0, NBLK - 1), k)
                v.wait_ge(x_final, NBLK * (b + 1))

            v.wait_ge(x_loaded[0], 16)
            normalise(norm_at(0, 0), pieces(xs, 0))
            v.wait_ge(pool_consts, QUADS_CLEARED)
            two_quads(0, 0)
            v.wait_ge(x_loaded[1], 16)
            normalise(norm_at(0, 1), pieces(xs, 1))
            v.wait_ge(bias_spread, 1)
            step(v.tensor_copy(off_b_all[:, :, :].rearrange("p d c -> p (d c)")[:, 0:OFFS + 2 * TAPS],
                               psum[:, SAMPLES, 0:OFFS + 2 * TAPS]))
            v.wait_ge(pool_consts, POOL_CONSTS + 1)
            corners(0, 0)
            indices(0, 0)
            hat_weights(0)
            grouped_pairs(0, [[lambda: two_quads(0, 1)], [], [], [lambda: corners(0, 1)],
                              [lambda: indices(0, 1)], [lambda: hat_weights(1)]])
            grouped_pairs(1, [[], [lambda: conv_block_stats(0, (0, 0, 0))]])
            conv_block_stats(1, (0, 0, NBLK - 1))
            v.wait_ge(conv_stat, B * NBLK)
            normalise(norm_at(0, B), [], (col[:, 0:1], col[:, 1:2]),
                      conv_stats[:, :].rearrange("p (j k) -> p j k", k=6))
            for b in range(B):
                last = v.tensor_copy(bn_affine[C * b:C * b + C, :], norm[:, norm_at(0, B), :])
            last.then_inc(affine_ready, 1)
            v.wait_ge(l1w_tanh, 1)
            step(v.tensor_tensor(l1_tmp[:, 3, :], l1_tmp[:, 2, :], l1_tmp[:, 1, :], ALU.subtract))
            for q in range(4):
                v.tensor_tensor(l1_sb[C * q:C * q + C, 0, :], l1_tmp[:, 3, :], l1_tmp[:, 1, :], ALU.add)
                last = v.tensor_copy(l1_sb[C * q:C * q + C, 1, :], l1_tmp[:, 0, :])
            last.then_inc(l1w_ready, 1)
            for q in range(4):
                here = slice(N // 4 * q, N // 4 * (q + 1))
                v.wait_ge(bn_out, q + 1)
                step(v.tensor_tensor(xs[:, 0, here], xs[:, 0, here], ys[:, 0, here], ALU.add))
                for j in (2 * q, 2 * q + 1):
                    block_stats(0, j)
            l1_normed(0)
            l1_sign_ste(0)
            l1_add_out(0)
            two_quads(1, 0)
            corners(1, 0)
            indices(1, 0)
            pairs(1, 0, [[lambda: add_relu(1), lambda: l1_normed(1)], [], [lambda: l1_sign_ste(1)],
                         [lambda: l1_add_out(1)],
                         [lambda: two_quads(1, 1)], [], [], [lambda: corners(1, 1)], [lambda: indices(1, 1)], []])
            first = (0, 0, 0)
            pairs(1, 1, [[l3_normed, l3_split],
                         [lambda: largest(0, first, range(0, 8))],
                         [lambda: largest(0, first, range(8, 20))],
                         [lambda: largest(0, first, range(20, CHUNK_N)), lambda: negated(0, first),
                          lambda: maxima_row(0, first)]])
            attention(0)
            attention(1)

        @block.scalar
        def _(act):
            act.wait_ge(pool_consts, QUADS_CLEARED)

            def deviation(n):
                act.wait_ge(var_ready, n + 1)
                act.activation(mv[:, n, 2:3], mv[:, n, 1:2], ACT.Sqrt, bias=eps[:, :]).then_inc(dev_ready, 1)

            def other_quads(d, b):
                n = norm_at(2 * d, b)
                if (d, b) != (0, 1):
                    deviation(n)
                else:
                    act.wait_ge(pool_consts, POOL_CONSTS + 1)
                act.wait_ge(norm_ready, n + 1)
                for q in (2, 3) if b else (2,):
                    quad_write(act.activation, q, d, b, on_scalar=True).then_inc(quads_ready, 1)

            def relu_of(b):
                s = bn_affine[C * b:C * b + C, :]
                return {"scale": s[:, 0:1], "bias": s[:, 1:2]}

            def copy_offsets(d, b):
                ph = phase(d, b)
                wait(act, indexed, ph)
                for h in range(2):
                    act.wait_ge(convs, 2 * ph + h + 1)
                    act.activation(flat_offs[:, h, :], psum[:, FREE + h, :], ACT.Identity).then_inc(convs_copied, 1)

            def masks(b):
                act.wait_ge(offs_ready, b + 1)
                o = offs[:, 0:TILES * OFFS].rearrange("p (t c) -> p t c", c=OFFS)[:, :, 2 * TAPS:]
                act.activation(o, o, ACT.Sigmoid).then_inc(mask_ready, 1)

            def rows(d, b):
                ph = phase(d, b)
                if ph:
                    act.wait_ge(rows_stored[(ph - 1) // B][(ph - 1) % B], 48)
                    if ph <= B:
                        act.wait_ge(padded_stored[ph - 1], 80)
                for g in range(9):
                    act.wait_ge(rows_turned, 9 * ph + g + 1)
                    m = min(4, QTILES - 4 * g)
                    act.activation(quad_rows[:, 4 * g:4 * g + m, :].rearrange("p t e -> p (t e)"),
                                   psum[:, SCORES + (9 * ph + g) % 2, 0:m * P], ACT.Identity).then_inc(rows_copied, 1)

            def tile(d, b, pair, u):
                n = tile_no(d, b, pair, u)
                act.wait_ge(turned, lin(n, 1, 1))
                act.activation(vals[:, u, :], psum[0:3 * C, sample_bank(d, u), 0:3 * P], ACT.Identity)\
                    .then_inc(vals_ready, 1)

            def finish(b, pair, u):
                n = tile_no(0, b, pair, u)
                act.wait_ge(outs, lin(n, 1, 1))
                var, stp, start = pair
                at = lin((var, 2 * stp, 2 * start + u), P)
                here = slice(at, at + P) if isinstance(at, int) else bass.ds(at, P)
                act.activation(conv_sums[b][:, here], psum[0:C, sample_bank(0, u), 3 * P:4 * P], ACT.Identity)\
                    .then_inc(outs_read, 1)

            def do_pair(d, b, pair):
                for u in range(2):
                    tile(d, b, pair, u)
                if d == 0:
                    for u in range(2):
                        finish(b, pair, u)

            def pairs(d, b, beside):
                for i in range(len(beside)):
                    do_pair(d, b, pair_of(i))
                    for work in beside[i]:
                        work()
                if (d, b) != (1, 1):
                    act.preload_act_table(ACT.Identity)
                    with act.Fori(len(beside), PAIRS) as i:
                        do_pair(d, b, pair_of(i))

            def load_window(b, group, u):
                var, stp, start = group
                for half in range(2):
                    first = lin((var, 4 * stp, 4 * start + u), 2 * PITCH * C,
                                (LEAD - 2 * PITCH - 2 + half * PITCH) * C)
                    src = bass.AP(padded[b].tensor, first, [[C, W], [PITCH * C, WINDOW], [1, WINDOW * C]])
                    act.dma_start(windows[W * half:W * half + W, u, :, :], src).then_inc(window_loads[u], 16)

            def grouped_pairs(b, beside):
                def windowed_pair(group, nxt_b, nxt):
                    for u in range(2):
                        pair = (group[0], 2 * group[1], 2 * group[2])
                        tile(0, b, pair, u)
                        if nxt is not None:
                            load_window(nxt_b, nxt, u)
                    for u in range(2):
                        finish(b, pair, u)

                if b == 0:
                    act.wait_ge(padded_stored[0], 80)
                    for u in range(2):
                        load_window(0, (0, 0, 0), u)
                for i in range(len(beside)):
                    if i % 2:
                        do_pair(0, b, pair_of(i))
                    else:
                        windowed_pair((0, 0, i // 2), b, (0, 0, i // 2 + 1))
                    for job in beside[i]:
                        job()
                act.preload_act_table(ACT.Identity)
                with act.Fori(len(beside) // 2, GROUPS - 1) as i:
                    windowed_pair((i, 1, 0), b, (i, 1, 1))
                    do_pair(0, b, (i, 2, 1))
                if b == 0:
                    act.wait_ge(padded_stored[1], 80)
                windowed_pair((0, 0, GROUPS - 1), b + 1, (0, 0, 0) if b == 0 else None)
                do_pair(0, b, pair_of(PAIRS - 1))

            def l1_tanh_and_sign(b):
                act.wait_ge(l1_g, b + 1)
                act.activation(l1_tanh_q, l1_normed_q, ACT.Tanh, scale=alpha[:, 0:1])
                act.activation(l1_sign_q, l1_normed_q, ACT.Sign).then_inc(l1_tanh, 1)

            def high_part(b, j):
                act.wait_ge(f_mm, NBLK * b + j + 1)
                act.activation(parts[:, 0, BLK * j:BLK * j + BLK], psum[0:2 * C, split_bank(b, j), :], ACT.Identity)
                act.activation(f3_flat[:, BLK * j:BLK * j + BLK], psum[2 * C:3 * C, split_bank(b, j), :],
                               ACT.Identity).then_inc(f_hi, 1)

            def l3_high():
                act.wait_ge(rows_stored[DEFORMS - 1][B - 1], 48)
                for j in range(NBLK):
                    high_part(0, j)
                act.wait_ge(g3_ready, 1)
                act.activation(xs[:, 0, :], xs[:, 0, :], ACT.Identity, scale=one_more[:, 0:1],
                               bias=norm[:, norm_at(3, 0), 1:2]).then_inc(residuals, 1)

            def prepare_image_1(j, s):
                n = norm_at(3, 1)
                quarter = slice(N // 4 * (s % 4), N // 4 * (s % 4 + 1))
                if (j, s) == (NBLK - 2, 1):
                    deviation(n)
                if j == NBLK - 2 and 4 <= s < 8:
                    act.wait_ge(norm_ready, n + 1)
                    act.activation(g3[1][0:C, quarter], xs[:, 1, quarter], ACT.Identity, scale=norm[:, n, 0:1],
                                   bias=norm[:, n, 1:2]).then_inc(g3_ready, 1)
                if (j, s) == SPLIT_AT[0]:
                    for sent, dmas in ((spread_a[0], 8), (spread_b[0], 4)):
                        act.wait_ge(sent, 16 * dmas)
                if (j, s) in SPLIT_AT:
                    high_part(1, SPLIT_AT.index((j, s)))
                if j == NBLK - 1 and 4 <= s < 8:
                    act.wait_ge(g3_ready, 5)
                    act.activation(xs[:, 1, quarter], xs[:, 1, quarter], ACT.Identity, scale=one_more[:, 1:2],
                                   bias=norm[:, n, 1:2]).then_inc(residuals, 1)

            def copy_sums(b, j):
                var, stp, start = j
                act.wait_ge(summed, lin((var, stp, start + NBLK * b), KEY_PAIRS, KEY_PAIRS))
                act.activation(att_halves, psum[:, SUMS, :], ACT.Identity).then_inc(sums_copied, 1)

            def attend(b, j, first=False, tiles=False, prepare=None):
                var, stp, start = j
                for s in range(KEY_PAIRS):
                    n = (var, KEY_PAIRS * stp, KEY_PAIRS * (start + NBLK * b) + s)
                    act.wait_ge(scored, lin(n, 1, 1))
                    wait(act, summed, lin(n, 1, -1))
                    act.activation(probs[:, s % 2, :],
                                   psum[:, SCORES + 2 * (s % 2):SCORES + 2 * (s % 2) + 2, :]
                                   .rearrange("p a n -> p (a n)"), ACT.Exp).then_inc(probs_ready, 1)
                    if s == 0 and not first:
                        copy_sums(b, (var, stp, start - 1))
                    if prepare is not None:
                        prepare(s)
                    if tiles and s % 4 == 2:
                        tile(1, 1, *merged_pair(j, s // 4))

            def attention(b):
                joint = MERGED if b == 0 else 0
                act.preload_act_table(ACT.Exp)
                attend(b, (0, 0, 0), first=True, tiles=joint > 0)
                if joint:
                    with act.Fori(1, joint) as j:
                        attend(b, (j, 1, 0), tiles=True)
                if b == 0:
                    assert joint == NBLK - 2
                    for j in range(joint, NBLK):
                        attend(b, (0, 0, j),
                               prepare=lambda s, j=j: prepare_image_1(j, s))
                else:
                    with act.Fori(1, NBLK - 1) as j:
                        attend(b, (j, 1, 0))
                    attend(b, (0, 0, NBLK - 1))
                act.wait_ge(sum_steps, SUM_STEPS * (NBLK * (b + 1) - 2) + 2)
                copy_sums(b, (0, 0, NBLK - 1))

            other_quads(0, 0)
            deviation(norm_at(0, 1))
            copy_offsets(0, 0)
            masks(0)
            rows(0, 0)
            grouped_pairs(0, [[lambda: other_quads(0, 1)], [lambda: copy_offsets(0, 1)], [],
                              [lambda: masks(1), lambda: rows(0, 1)], [], []])
            grouped_pairs(1, [])
            n = norm_at(0, B)
            deviation(n)
            act.activation(l1_tmp[:, 1, :], l1_tmp[:, 0, :], ACT.Tanh, scale=alpha[0:C, 1:2])
            act.activation(l1_tmp[:, 2, :], l1_tmp[:, 0, :], ACT.Sign).then_inc(l1w_tanh, 1)
            act.wait_ge(affine_ready, 1)
            for q in range(4):
                here = slice(N // 4 * q, N // 4 * (q + 1))
                act.activation(ys[:, 0, here], conv_sums[0][:, here], ACT.Relu, **relu_of(0)).then_inc(bn_out, 1)
            deviation(norm_at(1, 0))
            l1_tanh_and_sign(0)
            act.activation(ys[:, 1, :], conv_sums[1], ACT.Relu, **relu_of(1)).then_inc(bn_out, 1)
            other_quads(1, 0)
            copy_offsets(1, 0)
            rows(1, 0)
            pairs(1, 0, [[lambda: deviation(norm_at(1, 1))], [lambda: l1_tanh_and_sign(1)], [], [],
                         [lambda: other_quads(1, 1)], [lambda: copy_offsets(1, 1)], [], [lambda: rows(1, 1)], []])
            pairs(1, 1, [[lambda: deviation(norm_at(3, 0)), l3_high], [], [], []])
            attention(0)
            attention(1)

        @block.tensor
        def _(pe):
            pe.wait_ge(consts_loaded, N_CONST)
            pe.wait_ge(pool_consts, QUADS_CLEARED)
            pe.wait_ge(ident_made, 2)
            pe.matmul(psum[:, SAMPLES, 0:OFFS + 2 * TAPS], ones[0:1, :],
                      off_b_row[:, :, :].rearrange("p d c -> p (d c)")[:, 0:OFFS + 2 * TAPS],
                      start=True, stop=True).then_inc(bias_spread, 1)

            def offsets(d, b):
                ph = phase(d, b)
                pe.wait_ge(quads_ready, 4 * (ph + 1))
                wait(pe, offs_ready, ph)
                grid = quads[:, b, 0:GRID * PITCH].rearrange("p (y x) -> p y x", x=PITCH)
                for h in range(2):
                    for s, (sy, sx, _) in enumerate(SHIFTS):
                        for g in range(4):
                            y = 8 * (4 * h + g) + sy
                            last = pe.matmul(psum[C * g:C * g + C, FREE + h, :].rearrange("p (y x) -> p y x", x=W),
                                             off_w_sb[d][:, s, :], grid[:, y:y + 8, sx:sx + W],
                                             start=s == 0, stop=s == 3)
                    last.then_inc(convs, 1)

            def turn_offsets(d, b):
                for h in range(2):
                    pe.wait_ge(convs_copied, 2 * phase(d, b) + h + 1)
                    for t in range(4):
                        last = pe.transpose(psum[:, FREE + h, P * t:P * t + P], flat_offs[:, h, P * t:P * t + P],
                                            ident[:, :])
                    last.then_inc(convs_turned, 1)

            def turn_reach(b):
                pe.wait_ge(reach_ready, b + 1)
                pe.transpose(psum[0:1, FREE, 0:P], reach[:, b:b + 1], ident[:, :]).then_inc(reach_turned, 1)

            def rows(d, b):
                ph = phase(d, b)
                for g in range(9):
                    wait(pe, rows_copied, 9 * ph + g - 1)
                    for t in range(4 * g, min(4 * g + 4, QTILES)):
                        last = pe.transpose(psum[:, SCORES + (9 * ph + g) % 2, P * (t - 4 * g):P * (t - 4 * g) + P],
                                            quads[:, b, P * t:P * t + P], ident[:, :])
                    last.then_inc(rows_turned, 1)

            def turn(d, b, pair, u):
                n = tile_no(d, b, pair, u)
                pe.wait_ge(samples, lin(n, 1, 1))
                wait(pe, outs_read, lin(n, 1, d - 1))
                for g in range(3):
                    last = pe.transpose(psum[0:3 * C, sample_bank(d, u), P * g:P * g + P],
                                        sampled[:, u, 3 * C * g:3 * C * g + 3 * C], ident[:, :])
                last.then_inc(turned, 1)

            def sum_and_turn(b, pair, u):
                n = tile_no(0, b, pair, u)
                pe.wait_ge(samples, lin(n, 1, 1))
                wait(pe, outs_read, lin(n, 1, -1))
                for g in range(3):
                    for term in (0, 1, 2, 3, 8):
                        at = TAPS * C * term + 3 * C * g
                        last = pe.matmul(psum[0:3 * C, sample_bank(0, u), P * g:P * g + P],
                                         products[:, u, at:at + 3 * C], ident[:, :], start=term == 0, stop=term == 8)
                last.then_inc(turned, 1)

            def convolve(d, b, pair, u):
                n = tile_no(d, b, pair, u)
                pe.wait_ge(vals_ready, lin(n, 1, 1))
                for g in range(3):
                    last = pe.matmul(psum[0:C, sample_bank(d, u), 3 * P:4 * P], conv_w_sb[d][:, g, :],
                                     vals[:, u, P * g:P * g + P], start=g == 0, stop=g == 2)
                last.then_inc(outs, 1)

            def do_pair(d, b, pair):
                for u in range(2):
                    turn(d, b, pair, u)
                    if d:
                        convolve(d, b, pair, u)
                if d == 0:
                    for u in range(2):
                        convolve(d, b, pair, u)

            def windowed_pair(b, pair):
                for u in range(2):
                    sum_and_turn(b, pair, u)
                for u in range(2):
                    convolve(0, b, pair, u)

            def grouped_pairs(b, beside):
                for i in range(len(beside)):
                    if i % 2:
                        do_pair(0, b, pair_of(i))
                    else:
                        windowed_pair(b, pair_of(i))
                    for job in beside[i]:
                        job()
                with pe.Fori(len(beside) // 2, GROUPS) as i:
                    windowed_pair(b, (i, 2, 0))
                    do_pair(0, b, (i, 2, 1))

            def pairs(d, b, beside):
                for i in range(len(beside)):
                    do_pair(d, b, pair_of(i))
                    for work in beside[i]:
                        work()
                if (d, b) != (1, 1):
                    with pe.Fori(len(beside), PAIRS) as i:
                        do_pair(d, b, pair_of(i))

            def l1_products(b):
                pe.wait_ge(l1w_ready, 1)
                pe.wait_ge(l1_signs, b + 1)
                for h in range(2):
                    here = slice(BLK * h, BLK * h + BLK)
                    for k, src in enumerate((l1_normed_q, l1_sign_q)):
                        for q in range(4):
                            mine = slice(C * q, C * q + C)
                            last = pe.matmul(psum[mine, FREE + h, :], l1_sb[mine, k, :], src[mine, here],
                                             start=k == 0, stop=k == 1)
                    last.then_inc(l1_mm, 1)

            def project(b, j):
                pe.matmul(psum[0:3 * C, split_bank(b, j), :], w123_sb[:, :], g3[b][0:C + 1, BLK * j:BLK * j + BLK],
                          start=True, stop=True).then_inc(f_mm, 1)

            def l3_projections():
                pe.wait_ge(g3_ready, 1)
                pe.wait_ge(rows_copied, 9 * 2 * B)
                for j in range(NBLK):
                    if j >= 4:
                        pe.wait_ge(f_rem, j - 3)
                    project(0, j)
                for h in range(4):
                    turn_values(0, h)

            def turn_values(b, h):
                pe.wait_ge(f_hi, NBLK * b + 2 * h + 2)
                wait(pe, f3_ready, 5 * b + h - 1)
                here = slice(2 * C, 3 * C)
                for t in range(8):
                    at = P * (8 * h + t)
                    last = pe.transpose(psum[:, values_bank(b, h), C * t:C * t + C], f3_flat[:, at:at + P],
                                        ident[here, here])
                last.then_inc(f3_turned, 1)

            def prepare_image_1(j, s):
                if (j, s) in SPLIT_AT:
                    m = SPLIT_AT.index((j, s))
                    pe.wait_ge(g3_ready, 2 + m // 2)
                    if m:
                        pe.wait_ge(f_rem, NBLK + m)
                    else:
                        pe.wait_ge(outs_read, TILES * B * DEFORMS)
                    project(1, m)
                if (j, s) in VALUES_AT:
                    pe.wait_ge(f_rem, 2 * NBLK)
                    turn_values(1, VALUES_AT.index((j, s)))

            def score_chunks(b, j, chunks):
                var, stp, start = j
                n = (var, stp * CHUNK_N, (start + NBLK * b) * CHUNK_N)
                for c in chunks:
                    wait(pe, maxed, lin(n, 1, c - 1))
                    at = lin((var, 4 * stp, 4 * start + c // NBLK), P)
                    tile_of_q = slice(at, at + P) if isinstance(at, int) else bass.ds(at, P)
                    pe.matmul(psum[:, FREE + c % 2, :], qa[b][:, tile_of_q],
                              ka[b][:, BLK * (c % NBLK):BLK * (c % NBLK) + BLK], start=True, stop=True)\
                        .then_inc(chunk_scored, 1)

            def turn_maxima(b, j):
                var, stp, start = j
                pe.wait_ge(nm_ready, lin((var, stp, start + NBLK * b), 1, 1))
                for t in range(4):
                    last = pe.matmul(psum[2 * C:2 * C + SPLITS, FREE, P * t:P * t + P], nm_parts[:, t, :],
                                     ident_h[:, :], start=True, stop=True)
                last.then_inc(nm_mm, 1)

            def weigh(b, j, s):
                var, stp, start = j
                n = (var, KEY_PAIRS * stp, KEY_PAIRS * (start + NBLK * b) + s)
                pe.wait_ge(probs_ready, lin(n, 1, 1))
                for h in range(2):
                    last = pe.matmul(psum[2 * C * h:2 * C * h + 2 * C, SUMS, :], f3[b][:, 2 * s + h, :],
                                     probs[:, s % 2, BLK * h:BLK * h + BLK], start=s == 0, stop=s == KEY_PAIRS - 1)
                last.then_inc(summed, 1)

            def attend(b, j, first=False, last=False, tiles=False, prepare=None):
                var, stp, start = j
                nxt, prev = (var, stp, start + 1), (var, stp, start - 1)
                at = lin(j, BLK)
                here = slice(at, at + BLK) if isinstance(at, int) else bass.ds(at, BLK)
                rows_b = 2 * C + SPLITS
                if last and b == 0:
                    b_next, nxt, chunks = 1, (0, 0, 0), LAST_CHUNKS
                elif last:
                    b_next, chunks = b, [0] * KEY_PAIRS
                else:
                    b_next, chunks = b, MERGED_CHUNKS if tiles else CHUNKS
                more = sum(chunks) > 0
                c = 0
                for s in range(KEY_PAIRS):
                    n = (var, KEY_PAIRS * stp, KEY_PAIRS * (start + NBLK * b) + s)
                    wait(pe, probs_ready, lin(n, 1, -1))
                    keys = [slice(P * (2 * s + h), P * (2 * s + h) + P) for h in range(2)]
                    dst = [psum[:, SCORES + 2 * (s % 2) + h, :] for h in range(2)]
                    for h in range(2):
                        pe.matmul(dst[h], ka[b][:, keys[h]], qa[b][:, here], start=True, stop=False)
                    if s == 0:
                        pe.wait_ge(nm_rows, lin((var, stp, start + NBLK * b), 1, 1))
                    for h in range(2):
                        done = pe.matmul(dst[h], kb[0:rows_b, keys[h]], qb[0:rows_b, here], start=False, stop=True)
                    done.then_inc(scored, 1)
                    if s == KEY_PAIRS - 1 and more and not last:
                        turn_maxima(b, nxt)
                    m = chunks[s]
                    ahead = min(m, max(1, m // 2))
                    if m and c == 0 and b_next != b:
                        pe.wait_ge(spread_a[1], 16 * 8)
                    if m:
                        score_chunks(b_next, nxt, range(c, c + ahead))
                    if s:
                        if s == 1:
                            wait(pe, sums_copied, lin((var, stp, start + NBLK * b)))
                        weigh(b, j, s - 1)
                    elif not first:
                        weigh(b, prev, KEY_PAIRS - 1)
                    if m:
                        score_chunks(b_next, nxt, range(c + ahead, c + m))
                    c += m
                    if prepare is not None:
                        prepare(s)
                    if s == KEY_PAIRS - 1 and more and last:
                        turn_maxima(b_next, nxt)
                    if tiles and s % 4 == 2:
                        turn(1, 1, *merged_pair(j, s // 4))
                    if tiles and s % 4 == 3:
                        convolve(1, 1, *merged_pair(j, s // 4))

            def attention(b):
                joint = MERGED if b == 0 else 0
                pe.wait_ge(spread_b[b], 16 * 4)
                pe.wait_ge(f3_ready, 4 * (b + 1))
                attend(b, (0, 0, 0), first=True, tiles=joint > 0)
                if joint:
                    with pe.Fori(1, joint) as j:
                        attend(b, (j, 1, 0), tiles=True)
                if b == 0:
                    assert joint == NBLK - 2
                    for j in range(joint, NBLK):
                        attend(b, (0, 0, j), last=j == NBLK - 1,
                               prepare=lambda s, j=j: prepare_image_1(j, s))
                else:
                    with pe.Fori(1, NBLK - 1) as j:
                        attend(b, (j, 1, 0))
                    attend(b, (0, 0, NBLK - 1), last=True)
                weigh(b, (0, 0, NBLK - 1), KEY_PAIRS - 1)

            first = (0, 0, 0)
            offsets(0, 0)
            turn_offsets(0, 0)
            rows(0, 0)
            turn_reach(0)
            grouped_pairs(0, [[], [lambda: offsets(0, 1)], [lambda: turn_offsets(0, 1)], [lambda: rows(0, 1)],
                              [], [lambda: turn_reach(1)]])
            grouped_pairs(1, [])
            l1_products(0)
            offsets(1, 0)
            turn_offsets(1, 0)
            rows(1, 0)
            pairs(1, 0, [[], [], [], [lambda: l1_products(1)], [], [lambda: offsets(1, 1)],
                         [lambda: turn_offsets(1, 1)], [lambda: rows(1, 1)], []])
            pairs(1, 1, [[l3_projections],
                         [lambda: pe.wait_ge(f3_ready, 4), lambda: pe.wait_ge(spread_a[0], 16 * 8),
                          lambda: score_chunks(0, first, range(0, 8))],
                         [lambda: score_chunks(0, first, range(8, 20))],
                         [lambda: score_chunks(0, first, range(20, CHUNK_N)), lambda: turn_maxima(0, first)]])
            attention(0)
            attention(1)


def kernel(**inputs):
    import numpy as np
    import concourse.bacc as bacc
    from concourse.bass_utils import run_bass_kernel_spmd

    a = {k: np.asarray(v) for k, v in inputs.items()}
    off = np.concatenate([a["L0_conv_off_w"], a["L0_conv_mask_w"]], axis=0)
    arrays = {
        "x": a["x"],
        "off_w": off.transpose(2, 3, 1, 0),
        "off_b": np.concatenate([a["L0_conv_off_b"], a["L0_conv_mask_b"]])[None, :],
        "conv_w": a["L0_conv_conv_w"].transpose(2, 3, 1, 0).reshape(3, 3 * C, C),
        "gamma": a["L0_conv_gamma"][:, None], "beta": a["L0_conv_beta"][:, None],
        "l1_w": a["L1_conv_weight"].reshape(C, C).T,
        "l1_ax": a["L1_conv_alpha_x"].reshape(1, 1), "l1_aw": a["L1_conv_alpha_w"].reshape(1, 1),
        "off2_w": a["L2_conv_offset_w"].transpose(2, 3, 1, 0), "off2_b": a["L2_conv_offset_b"][None, :],
        "conv2_w": a["L2_conv_deform_w"].transpose(2, 3, 1, 0).reshape(3, 3 * C, C),
        "conv2_b": a["L2_conv_deform_b"][:, None],
        "w123": np.concatenate([a[f"L3_conv_w{k}"].T for k in (1, 2, 3)], axis=1),
        "b123": np.concatenate([a[f"L3_conv_b{k}"] for k in (1, 2, 3)])[None, :],
    }
    nc = bacc.Bacc("TRN2", target_bir_lowering=False, num_devices=1)
    fed, args = {}, []
    for name, v in arrays.items():
        v = np.ascontiguousarray(v)
        fed[f"in_{name}"] = v
        args.append(nc.dram_tensor(f"in_{name}", v.shape, mybir.dt.from_np(v.dtype), kind="ExternalInput").ap())
    args.append(nc.dram_tensor("out_x", (B, C, H, W), F32, kind="ExternalOutput").ap())
    build(nc, *args)
    r = run_bass_kernel_spmd(nc, [fed], core_ids=[0])
    return r.results[0]["out_x"]
```
